# Optimizing a Trainium2 kernel written in Bass

```python
import numpy as np
import jax
import jax.numpy as jnp

def _softmax(x, axis=-1):
    return jax.nn.softmax(x, axis=axis)

def _gelu(x):
    return jax.nn.gelu(x, approximate=True)

def _silu(x):
    return jax.nn.silu(x)

def _sigmoid(x):
    return jax.nn.sigmoid(x)

def _layernorm(x, axis=-1, eps=1e-05):
    m = jnp.mean(x, axis=axis, keepdims=True)
    v = jnp.var(x, axis=axis, keepdims=True)
    return (x - m) / jnp.sqrt(v + eps)

def _scatter_add(tgt, idx, src, axis=0):
    return tgt.at[idx].add(src)

def _segment_sum(src, seg, n):
    return jax.ops.segment_sum(src, seg, n)
kernel_name = 'mk_adj_resnorm_d1_adj_r2_4248be'

def setup_inputs(seed: int=0):
    np.random.seed(seed)
    _w = jnp.asarray

    def _rec_inputs():
        import jax
        import jax.numpy as jnp
        _gk = jax.random.key(seed)
        x = 7.22e-05 + 1 * jax.random.normal(jax.random.fold_in(_gk, 1), (32, 256, 256), jnp.float32)
        _a = jax.random.bernoulli(jax.random.fold_in(_gk, 2), 0.0078125, (32, 256, 256))
        _a = jnp.logical_or(_a, jnp.swapaxes(_a, -1, -2))
        _a = jnp.logical_or(_a, jnp.eye(256, dtype=bool))
        _af = _a.astype(jnp.float32)
        _af = _af * jax.random.uniform(jax.random.fold_in(_gk, 3), (32, 256, 256), jnp.float32, 0.05, 1)
        adj = _af
        return (x, adj)
    x, adj = _rec_inputs()

    def _L0_gnn_setup():
        import jax, jax.numpy as jnp
        import numpy as np
        EPS_LN = 1e-05

        def hypergraph_conv(x, adj, W, b):
            N, C, _ = adj.shape
            H = (adj != 0).astype(x.dtype)
            w = adj.reshape(N, -1)[:, :C]
            xw = jnp.einsum('ncd,hd->nch', x, W)
            Dn = jnp.einsum('nce,ne->nc', H, w)
            Dn = jnp.where(Dn > 0, 1.0 / Dn, 0.0)
            Be = H.sum(axis=1)
            Be = jnp.where(Be > 0, 1.0 / Be, 0.0)
            m = Be[:, :, None] * jnp.einsum('nce,nch->neh', H, xw)
            out = Dn[:, :, None] * jnp.einsum('nce,neh->nch', H, m)
            return out + b

        def layer_norm(x, g, b):
            mu = jnp.mean(x, axis=-1, keepdims=True)
            var = jnp.var(x, axis=-1, keepdims=True)
            return (x - mu) * jax.lax.rsqrt(var + EPS_LN) * g + b
        key = jax.random.key(seed)
        ks = jax.random.split(key, 4)
        N, C, Din, Dh, Dout = (16, 512, 256, 512, 256)
        x = jax.random.normal(ks[0], (N, C, Din), dtype=jnp.float32)
        adj = jax.random.uniform(ks[1], (N, C, C), dtype=jnp.float32, minval=0.1, maxval=1.0)
        W1 = jax.random.normal(ks[2], (Dh, Din), dtype=jnp.float32) * (1.0 / np.sqrt(Din))
        b1 = jnp.zeros((Dh,), dtype=jnp.float32)
        gamma = jnp.ones((Dh,), dtype=jnp.float32)
        beta = jnp.zeros((Dh,), dtype=jnp.float32)
        W2 = jax.random.normal(ks[3], (Dout, Dh), dtype=jnp.float32) * (1.0 / np.sqrt(Dh))
        b2 = jnp.zeros((Dout,), dtype=jnp.float32)
        return {'x': x, 'adj': adj, 'W1': W1, 'b1': b1, 'gamma': gamma, 'beta': beta, 'W2': W2, 'b2': b2}
    _L0_gnn_all = _L0_gnn_setup()
    _L0_gnn_in = {k: v for k, v in _L0_gnn_all.items() if k in ('W1', 'b1', 'gamma', 'beta', 'W2', 'b2')}
    del _L0_gnn_all
    return {'x': x, 'adj': adj, 'L0_gnn_W1': _L0_gnn_in['W1'], 'L0_gnn_b1': _L0_gnn_in['b1'], 'L0_gnn_gamma': _L0_gnn_in['gamma'], 'L0_gnn_beta': _L0_gnn_in['beta'], 'L0_gnn_W2': _L0_gnn_in['W2'], 'L0_gnn_b2': _L0_gnn_in['b2']}

def reference(x, adj, L0_gnn_W1, L0_gnn_b1, L0_gnn_gamma, L0_gnn_beta, L0_gnn_W2, L0_gnn_b2):
    import jax
    import jax.numpy as jnp

    def _L0_gnn_ref(x, adj, W1, b1, gamma, beta, W2, b2):
        import jax, jax.numpy as jnp
        import numpy as np
        EPS_LN = 1e-05

        def hypergraph_conv(x, adj, W, b):
            N, C, _ = adj.shape
            H = (adj != 0).astype(x.dtype)
            w = adj.reshape(N, -1)[:, :C]
            xw = jnp.einsum('ncd,hd->nch', x, W)
            Dn = jnp.einsum('nce,ne->nc', H, w)
            Dn = jnp.where(Dn > 0, 1.0 / Dn, 0.0)
            Be = H.sum(axis=1)
            Be = jnp.where(Be > 0, 1.0 / Be, 0.0)
            m = Be[:, :, None] * jnp.einsum('nce,nch->neh', H, xw)
            out = Dn[:, :, None] * jnp.einsum('nce,neh->nch', H, m)
            return out + b

        def layer_norm(x, g, b):
            mu = jnp.mean(x, axis=-1, keepdims=True)
            var = jnp.var(x, axis=-1, keepdims=True)
            return (x - mu) * jax.lax.rsqrt(var + EPS_LN) * g + b
        h = jax.nn.relu(hypergraph_conv(x, adj, W1, b1))
        h = layer_norm(h, gamma, beta)
        y = hypergraph_conv(h, adj, W2, b2)
        return y + x
    x = _layernorm(x + _L0_gnn_ref(x, adj, L0_gnn_W1, L0_gnn_b1, L0_gnn_gamma, L0_gnn_beta, L0_gnn_W2, L0_gnn_b2), axis=-1)
    return x

_drawn_inputs = setup_inputs


def setup_inputs(seed=0):
    import zlib

    import numpy as np

    out = dict(_drawn_inputs(seed))
    spreads = {'L0_gnn_b1': (0.0, 0.1),
     'L0_gnn_gamma': (1.0, 0.2),
     'L0_gnn_beta': (0.0, 0.1),
     'L0_gnn_b2': (0.0, 0.1)}
    factors = {}
    for name, (base, spread) in spreads.items():
        noise = np.random.default_rng([zlib.crc32(name.encode()), seed]).standard_normal(out[name].shape)
        drawn = base * np.exp(spread * noise) if base else spread * noise
        out[name] = jnp.asarray(drawn.astype(out[name].dtype))
    for name, factor in factors.items():
        out[name] = (out[name] * factor).astype(out[name].dtype)
    return out
```

```python
from contextlib import ExitStack

import concourse.bass as bass
from concourse import mybir

ALU = mybir.AluOpType
ACT = mybir.ActivationFunctionType
F32 = mybir.dt.float32
F32R = mybir.dt.float32r

P = 128
EPS = 1e-5
TINY = 1.1754944e-38


def hypergraph_resnorm_kernel(nc, x, adj, W1, b1, gamma, beta, W2, b2, out):
    N, C, DI = x.shape
    DH = W1.shape[0]
    DO = W2.shape[0]
    CT, ET, DT, HT_, OT = C // P, C // P, DI // P, DH // P, DO // P
    assert C == 2 * P and DI == DO == 2 * P and DH == 4 * P and N % 2 == 0 and N >= 6

    x_rows = x.rearrange("n (p t) d -> n p t d", t=CT)
    adj_rows = adj.rearrange("n (p t) e -> n p t e", t=CT)
    out_rows = out.rearrange("n (p t) d -> n p t d", t=CT)

    with ExitStack() as ctx:
        def sb(name, shape, dt=F32):
            return ctx.enter_context(nc.sbuf_tensor(name, shape, dt))

        def bank(name, shape):
            return ctx.enter_context(nc.psum_tensor(name, shape, F32))

        def sem(name):
            return ctx.enter_context(nc.semaphore(name))

        ident = sb("ident", [P, P])
        inv_dh = sb("inv_dh", [P, P])
        ones = sb("ones", [P, P])
        eps = sb("eps", [P, 1])
        w1_in = sb("w1_in", [P, HT_, DI])
        w2_in = sb("w2_in", [P, OT, DH])
        gb_in = sb("gb_in", [2 * HT_, P])
        wrow_in = sb("wrow_in", [N, C])
        b1_all = sb("b1_all", [P, DH])
        b2_all = sb("b2_all", [P, CT, DO])
        gb_col = sb("gb_col", [P, 2 * HT_])
        beta_rep = sb("beta_rep", [P, HT_, P])
        edge_w = sb("edge_w", [P, ET, N, 2], F32R)
        w1_hi = sb("w1_hi", [P, DT, DH], F32R)
        w1_lo = sb("w1_lo", [P, DT, DH], F32R)
        w2_g = sb("w2_g", [P, HT_, DO])
        w2_t = sb("w2_t", [P, HT_, DO])
        w2_c = sb("w2_c", [P, HT_, DO])
        w2_hi = sb("w2_hi", [P, HT_, DO], F32R)
        w2_lo = sb("w2_lo", [P, HT_, DO], F32R)
        beta_w2 = sb("beta_w2", [P, DO])

        x_in = [sb(f"x_in{j}", [P, CT, DI]) for j in range(2)]
        adj_in = [sb(f"adj_in{j}", [P, CT, C]) for j in range(2)]
        res = [sb(f"res{j}", [P, CT, DO]) for j in range(2)]
        out_sb = [sb(f"out_sb{j}", [P, CT, DO]) for j in range(2)]
        a_hi = [sb(f"a_hi{j}", [P, CT, C], F32R) for j in range(2)]
        a_lo = [sb(f"a_lo{j}", [P, CT, C], F32R) for j in range(2)]
        node_inv = [sb(f"node_inv{j}", [P, CT]) for j in range(2)]

        ht = sb("ht", [P, ET, C], F32R)
        edge_n = sb("edge_n", [P, ET])
        edge_n1 = sb("edge_n1", [P, ET])
        edge_inv = sb("edge_inv", [P, ET])
        edge_inv_hi = sb("edge_inv_hi", [P, ET], F32R)
        edge_inv_lo = sb("edge_inv_lo", [P, ET])
        hb_hi = sb("hb_hi", [P, ET, C], F32R)
        hb_lo = sb("hb_lo", [P, ET, C], F32R)
        node_w = sb("node_w", [P, CT])
        node_w1 = sb("node_w1", [P, CT])
        node_r = sb("node_r", [P, CT])
        x_hi = sb("x_hi", [P, CT, DI], F32R)
        x_lo = sb("x_lo", [P, CT, DI], F32R)
        res_b = sb("res_b", [P, CT, DO])
        p_hi = sb("p_hi", [P, DT, C], F32R)
        p_lo = sb("p_lo", [P, DT, C], F32R)
        v = sb("v", [P, CT, DH])
        r = sb("r", [P, CT, DH])
        st1 = sb("st1", [P, CT, 6])
        mv1 = sb("mv1", [P, CT, 2])
        sd1 = sb("sd1", [P, CT])
        rstd1 = sb("rstd1", [P, CT])
        r_hi = sb("r_hi", [P, HT_, C], F32R)
        r_lo = sb("r_lo", [P, HT_, C], F32R)
        y = sb("y", [P, CT, DO])
        y_hi = sb("y_hi", [P, CT, DO], F32R)
        y_lo = sb("y_lo", [P, CT, DO], F32R)
        t_sb = sb("t_sb", [P, CT, DO])
        st2 = sb("st2", [P, CT, 6])
        mv2 = sb("mv2", [P, CT, 2])
        sd2 = sb("sd2", [P, CT])
        rstd2 = sb("rstd2", [P, CT])
        shift2 = sb("shift2", [P, CT])

        zr = [bank(f"zr{k}", [P, 512]) for k in range(2)]
        ys = [bank(f"ys{t}", [P, 512]) for t in range(2)]
        ap_ = bank("ap", [P, 512])
        qs = bank("qs", [P, 512])
        ts = bank("ts", [P, 512])
        ds = bank("ds", [P, 512])
        z_ps = zr
        r_ps = [b[:, :].rearrange("p (k c) -> p k c", k=2) for b in zr]
        y_ps = [b[:, 0:DO] for b in ys]
        a_ps = ap_[:, :].rearrange("p (t c) -> p t c", t=CT)
        p_ps = ap_[:, :].rearrange("p (k c) -> p k c", k=DT)
        q_ps = qs[:, :].rearrange("p (t o) -> p t o", t=CT)
        t_ps = ts[:, :].rearrange("p (k c) -> p k c", k=ET)
        d_ps = ds[:, 0:2 * CT].rearrange("p (t h) -> p t h", t=CT)
        w1_ps = zr
        w2_ps = [b[:, :].rearrange("p (k o) -> p k o", k=2) for b in ys]
        gb_ps = ds[:, 0:2 * HT_]
        wcol_ps = ds[:, 64:64 + ET * N].rearrange("p (k n) -> p k n", k=ET)
        mean_ps = qs[:, 0:DO]
        beta_ps = qs[:, DO:2 * DO]

        s_small = sem("s_small_loaded")
        s_w1 = sem("s_w1_loaded")
        s_w2 = sem("s_w2_loaded")
        s_bias = sem("s_bias_loaded")
        s_zeroed = sem("s_zeroed")
        s_const = sem("s_const_made")
        s_gbT = sem("s_small_transposed")
        s_gb = sem("s_gamma_beta_copied")
        s_ewh = sem("s_edge_w_hi")
        s_ewl = sem("s_edge_w_lo")
        s_w1T = sem("s_w1_transposed")
        s_w1h = sem("s_w1_hi")
        s_w1l = sem("s_w1_lo")
        s_w2T = sem("s_w2_transposed")
        s_w2g = sem("s_w2_gamma")
        s_w2t = sem("s_w2_copied")
        s_brep = sem("s_beta_rep")
        s_w2m = sem("s_w2_means")
        s_w2c = sem("s_w2_centred")
        s_bw2 = sem("s_beta_w2")
        s_w2h = sem("s_w2_hi")
        s_w2l = sem("s_w2_lo")

        x_loaded = [sem(f"x_loaded{j}") for j in range(2)]
        adj_loaded = [sem(f"adj_loaded{j}") for j in range(2)]
        out_stored = [sem(f"out_stored{j}") for j in range(2)]
        T_done = sem("T_done")
        A_done = sem("A_done")
        D_done = sem("D_done")
        P_done = sem("P_done")
        Z_tile = sem("Z_tile")
        R_done = sem("R_done")
        Y_tile = sem("Y_tile")
        Q_done = sem("Q_done")
        ht_tile = sem("ht_tile")
        edge_n1_done = sem("edge_n1_done")
        edge_inv_done = sem("edge_inv_done")
        edge_hi_done = sem("edge_hi_done")
        edge_lo_done = sem("edge_lo_done")
        hb_hi_done = sem("hb_hi_done")
        hb_lo_done = sem("hb_lo_done")
        a_hi_done = sem("a_hi_done")
        a_lo_done = sem("a_lo_done")
        node_w_done = sem("node_w_done")
        node_w1_done = sem("node_w1_done")
        node_r_done = sem("node_r_done")
        node_inv_done = sem("node_inv_done")
        x_hi_done = sem("x_hi_done")
        x_lo_done = sem("x_lo_done")
        res_b_done = sem("res_b_done")
        res_done = sem("res_done")
        p_hi_done = sem("p_hi_done")
        p_lo_done = sem("p_lo_done")
        v_tile = sem("v_tile")
        r_tile = sem("r_tile")
        st1_tile = sem("st1_tile")
        mv1_tile = sem("mv1_tile")
        sd1_done = sem("sd1_done")
        rstd1_done = sem("rstd1_done")
        r_hi_tile = sem("r_hi_tile")
        r_lo_tile = sem("r_lo_tile")
        y_tile = sem("y_tile")
        y_hi_tile = sem("y_hi_tile")
        y_lo_tile = sem("y_lo_tile")
        t_tile = sem("t_tile")
        st2_tile = sem("st2_tile")
        mv2_tile = sem("mv2_tile")
        sd2_done = sem("sd2_done")
        rstd2_done = sem("rstd2_done")
        shift2_done = sem("shift2_done")
        out_tile = sem("out_tile")

        def known(m, j):
            return not isinstance(m, int) or 0 <= 2 * m + j < N

        def ones_(m, j):
            return 2 * m + (j + 1)

        def tiles(m, j, t):
            return 4 * m + (2 * j + t + 1)

        def loads(m, j):
            return 16 * m + 16 * (j // 2 + 1)

        def wait(eng, s, value):
            if not isinstance(value, int) or value > 0:
                eng.wait_ge(s, value)

        def run(eng, slot, setup=None, setup2=None, ahead=2):
            slot(-1, 0)
            if setup:
                setup()
            slot(-1, 1)
            if setup2:
                setup2()
            slot(0, 0)
            slot(0, 1)
            whole = (N - ahead) // 2
            with eng.Fori(1, whole) as m:
                slot(m, 0)
                slot(m, 1)
            for m in range(whole, N // 2):
                slot(m, 0)
                slot(m, 1)
            slot(N // 2, 0)

        block = ctx.enter_context(nc.Block())

        @block.sync
        def _(sp):
            def load_x(m, j):
                if known(m, j):
                    sp.dma_start(x_in[j % 2][:, :, :], x_rows[2 * m + j]).then_inc(x_loaded[j % 2], 16)

            def load_adj(m, j):
                if known(m, j):
                    sp.dma_start(adj_in[j % 2][:, :, :], adj_rows[2 * m + j]).then_inc(adj_loaded[j % 2], 16)

            load_adj(0, 0)
            sp.dma_start(wrow_in[:, :], adj[:, 0, :]).then_inc(s_small, 16)
            sp.dma_start(gb_in[0:HT_, :], gamma.rearrange("(k p) -> k p", p=P)).then_inc(s_small, 16)
            sp.dma_start(gb_in[HT_:2 * HT_, :], beta.rearrange("(k p) -> k p", p=P)).then_inc(s_small, 16)
            load_x(0, 0)
            load_adj(0, 1)
            sp.dma_start(w1_in[:, :, :], W1.rearrange("(k p) d -> p k d", p=P)).then_inc(s_w1, 16)
            sp.dma_start(w2_in[:, :, :], W2.rearrange("(k p) h -> p k h", p=P)).then_inc(s_w2, 16)
            load_x(0, 1)
            sp.dma_start(b1_all[:, :], b1.rearrange("(a h) -> a h", a=1).broadcast_to([P, DH])).then_inc(s_bias, 16)
            for t in range(CT):
                sp.dma_start(b2_all[:, t, :],
                             b2.rearrange("(a h) -> a h", a=1).broadcast_to([P, DO])).then_inc(s_bias, 16)

            def slot(m, j):
                if known(m, j + 4):
                    wait(sp, T_done, ones_(m, j + 2))
                    load_adj(m, j + 4)
                if known(m, j + 3) and known(m, j + 1):
                    wait(sp, x_hi_done, ones_(m, j + 1))
                    wait(sp, x_lo_done, ones_(m, j + 1))
                    wait(sp, res_done, ones_(m, j + 1))
                    load_x(m, j + 3)
                if known(m, j - 1):
                    wait(sp, out_tile, tiles(m, j - 1, 1))
                    sp.dma_start(out_rows[2 * m + (j - 1)], out_sb[(j - 1) % 2][:, :, :]) \
                      .then_inc(out_stored[(j - 1) % 2], 16)

            run(sp, slot, ahead=4)
            sp.wait_ge(out_stored[0], 16 * (N // 2))
            sp.wait_ge(out_stored[1], 16 * (N // 2))

        @block.tensor
        def _(pe):
            def products(out_, terms, done=None):
                for n, (lhs, rhs) in enumerate(terms):
                    ins = pe.matmul(out_, lhs, rhs, start=(n == 0), stop=(n == len(terms) - 1))
                return ins

            def transpose_adj(m, j):
                wait(pe, adj_loaded[j % 2], loads(m, j))
                wait(pe, ht_tile, tiles(m, j - 1, 1))
                for t in range(CT):
                    for k in range(ET):
                        ins = pe.transpose(t_ps[:, k, t * P:(t + 1) * P],
                                           adj_in[j % 2][:, t, k * P:(k + 1) * P], ident[:, :])
                ins.then_inc(T_done, 1)

            def build_a(m, j):
                wait(pe, p_lo_done, ones_(m, j - 1))
                wait(pe, hb_hi_done, ones_(m, j))
                for t in range(CT):
                    at = slice(t * P, (t + 1) * P)
                    for k in range(ET):
                        pe.matmul(a_ps[:, t, :], hb_hi[:, k, at], ht[:, k, :], start=(k == 0), stop=False)
                    if t == 0:
                        wait(pe, hb_lo_done, ones_(m, j))
                    for k in range(ET):
                        ins = pe.matmul(a_ps[:, t, :], hb_lo[:, k, at], ht[:, k, :], start=False,
                                        stop=(k == ET - 1))
                ins.then_inc(A_done, 1)

            def node_weights(m, j):
                wait(pe, node_w_done, ones_(m, j - 1))
                if not isinstance(m, int):
                    w = edge_w[:, :, bass.ds(2 * m + j, 1), :]
                else:
                    w = edge_w[:, :, 2 * m + j:2 * m + j + 1, :]
                for t in range(CT):
                    for k in range(ET):
                        ins = pe.matmul(d_ps[:, t, :], ht[:, k, t * P:(t + 1) * P], w[:, k, 0, :],
                                        start=(k == 0), stop=(k == ET - 1))
                ins.then_inc(D_done, 1)

            def aggregate_x(m, j):
                wait(pe, x_hi_done, ones_(m, j))
                wait(pe, a_hi_done, ones_(m, j))
                wait(pe, x_lo_done, ones_(m, j))
                wait(pe, a_lo_done, ones_(m, j))
                n = j % 2
                for k in range(DT):
                    at = slice(k * P, (k + 1) * P)
                    for i, (xs, as_) in enumerate(((x_hi, a_hi), (x_lo, a_hi), (x_hi, a_lo))):
                        for t in range(CT):
                            ins = pe.matmul(p_ps[:, k, :], xs[:, t, at], as_[n][:, t, :],
                                            start=(i == 0 and t == 0), stop=(i == 2 and t == CT - 1))
                ins.then_inc(P_done, 1)

            def hidden(m, j):
                wait(pe, p_hi_done, ones_(m, j))
                wait(pe, r_lo_tile, tiles(m, j - 1, 1))
                for t in range(CT):
                    at = slice(t * P, (t + 1) * P)
                    for i, (ps, ws) in enumerate(((p_hi, w1_hi), (p_hi, w1_lo), (p_lo, w1_hi))):
                        if i == 2 and t == 0:
                            wait(pe, p_lo_done, ones_(m, j))
                        for k in range(DT):
                            ins = pe.matmul(z_ps[t][:, :], ps[:, k, at], ws[:, k, :],
                                            start=(i == 0 and k == 0), stop=(i == 2 and k == DT - 1))
                    ins.then_inc(Z_tile, 1)

            def transpose_r(m, j):
                wait(pe, v_tile, tiles(m, j, 1))
                for t in range(CT):
                    wait(pe, r_tile, tiles(m, j, t))
                    for k in range(HT_):
                        ins = pe.transpose(r_ps[k // 2][:, k % 2, t * P:(t + 1) * P],
                                           r[:, t, k * P:(k + 1) * P], ident[:, :])
                ins.then_inc(R_done, 1)

            def project(m, j, t):
                wait(pe, y_tile, tiles(m, j - 1, t))
                at = slice(t * P, (t + 1) * P)
                if t == 0:
                    wait(pe, r_hi_tile, tiles(m, j, 1))
                for i, (rs, ws) in enumerate(((r_hi, w2_hi), (r_hi, w2_lo), (r_lo, w2_hi))):
                    if i == 2 and t == 0:
                        wait(pe, r_lo_tile, tiles(m, j, 1))
                    for k in range(HT_):
                        ins = pe.matmul(y_ps[t], rs[:, k, at], ws[:, k, :],
                                        start=(i == 0 and k == 0), stop=(i == 2 and k == HT_ - 1))
                ins.then_inc(Y_tile, 1)

            def aggregate_y(m, j):
                wait(pe, t_tile, tiles(m, j - 1, 1))
                wait(pe, y_hi_tile, tiles(m, j, 1))
                n = j % 2
                for t in range(CT):
                    at = slice(t * P, (t + 1) * P)
                    for i, (as_, yy) in enumerate(((a_hi, y_hi), (a_lo, y_hi), (a_hi, y_lo))):
                        if i == 2 and t == 0:
                            wait(pe, y_lo_tile, tiles(m, j, 1))
                        for k in range(CT):
                            ins = pe.matmul(q_ps[:, t, :], as_[n][:, k, at], yy[:, k, :],
                                            start=(i == 0 and k == 0), stop=(i == 2 and k == CT - 1))
                ins.then_inc(Q_done, 1)

            def setup():
                pe.wait_ge(s_small, 48)
                pe.transpose(gb_ps, gb_in[:, :], ident[0:2 * HT_, 0:2 * HT_])
                for k in range(ET):
                    ins = pe.transpose(wcol_ps[:, k, :], wrow_in[:, k * P:(k + 1) * P], ident[0:N, 0:N])
                ins.then_inc(s_gbT, 1)
                pe.wait_ge(s_w1, 16)
                for d in range(DT):
                    for k in range(HT_):
                        ins = pe.transpose(w1_ps[d][:, k * P:(k + 1) * P], w1_in[:, k, d * P:(d + 1) * P],
                                           ident[:, :])
                ins.then_inc(s_w1T, 1)
                pe.wait_ge(s_w2, 16)
                for k in range(HT_):
                    for o in range(OT):
                        ins = pe.transpose(w2_ps[k // 2][:, k % 2, o * P:(o + 1) * P],
                                           w2_in[:, o, k * P:(k + 1) * P], ident[:, :])
                ins.then_inc(s_w2T, 1)
                pe.wait_ge(s_ewl, 1)
                pe.wait_ge(s_gb, 1)

            def setup2():
                pe.wait_ge(s_w2g, HT_)
                products(mean_ps, [(inv_dh[:, :], w2_g[:, k, :]) for k in range(HT_)])
                pe.wait_ge(s_w2t, HT_)
                pe.wait_ge(s_brep, HT_)
                products(beta_ps, [(beta_rep[:, k, :], w2_t[:, k, :]) for k in range(HT_)]).then_inc(s_w2m, 1)
                pe.wait_ge(s_w1h, DT)
                pe.wait_ge(s_w1l, DT)
                pe.wait_ge(s_w2h, 1)
                pe.wait_ge(s_w2l, 1)
                pe.wait_ge(s_bw2, 1)

            def slot(m, j):
                if known(m, j):
                    hidden(m, j)
                if known(m, j - 1):
                    aggregate_y(m, j - 1)
                if known(m, j):
                    transpose_r(m, j)
                if known(m, j + 1):
                    build_a(m, j + 1)
                    node_weights(m, j + 1)
                if known(m, j + 2):
                    transpose_adj(m, j + 2)
                if known(m, j):
                    project(m, j, 0)
                if known(m, j + 1):
                    aggregate_x(m, j + 1)
                if known(m, j):
                    project(m, j, 1)

            pe.wait_ge(s_const, 2)
            run(pe, slot, setup, setup2)

        @block.vector
        def _(dve):
            def setup():
                dve.wait_ge(s_gbT, 1)
                dve.tensor_copy(gb_col[:, :], gb_ps).then_inc(s_gb, 1)
                dve.tensor_copy(edge_w[:, :, :, 0], wcol_ps).then_inc(s_ewh, 1)
                dve.wait_ge(s_ewh, 1)
                dve.tensor_tensor(edge_w[:, :, :, 1], wcol_ps, edge_w[:, :, :, 0].bitcast(F32),
                                  ALU.subtract).then_inc(s_ewl, 1)

            def setup2():
                for d in range(DT):
                    dve.wait_ge(s_w1h, d + 1)
                    dve.tensor_tensor(w1_lo[:, d, :], w1_ps[d][:, :], w1_hi[:, d, :].bitcast(F32),
                                      ALU.subtract).then_inc(s_w1l, 1)
                dve.wait_ge(s_w2T, 1)
                dve.wait_ge(s_gb, 1)
                dve.wait_ge(s_w2t, HT_)
                for k in range(HT_):
                    dve.tensor_scalar(w2_g[:, k, :], w2_ps[k // 2][:, k % 2, :], gb_col[:, k:k + 1], None,
                                      ALU.mult).then_inc(s_w2g, 1)
                dve.wait_ge(s_w2g, HT_)
                dve.wait_ge(s_w2m, 1)
                for k in range(HT_):
                    dve.tensor_tensor(w2_c[:, k, :], w2_g[:, k, :], mean_ps, ALU.subtract).then_inc(s_w2c, 1)
                dve.tensor_copy(beta_w2[:, :], beta_ps).then_inc(s_bw2, 1)
                dve.wait_ge(s_w2h, 1)
                dve.tensor_tensor(w2_lo[:, :, :], w2_c[:, :, :], w2_hi[:, :, :].bitcast(F32),
                                  ALU.subtract).then_inc(s_w2l, 1)

            def conv1_out(m, j, t):
                if t == 0:
                    wait(dve, node_inv_done, ones_(m, j))
                    wait(dve, R_done, ones_(m, j - 1))
                wait(dve, r_tile, tiles(m, j - 1, t))
                wait(dve, Z_tile, tiles(m, j, t))
                dve.scalar_tensor_tensor(v[:, t, :], z_ps[t][:, :], node_inv[j % 2][:, t:t + 1],
                                         b1_all[:, :], ALU.mult, ALU.add).then_inc(v_tile, 1)

            def stats1(m, j, t):
                wait(dve, r_tile, tiles(m, j, t))
                dve.bn_stats(st1[:, t, :], r[:, t, :]).then_inc(st1_tile, 1)

            def before_aggr1(m, j):
                wait(dve, st1_tile, tiles(m, j, 1))
                wait(dve, sd1_done, ones_(m, j - 1))

            def aggr1(m, j):
                for t in range(CT):
                    dve.bn_aggr(mv1[:, t, :], st1[:, t, :]).then_inc(mv1_tile, 1)

            def conv2_out(m, j, t):
                if t == 0:
                    wait(dve, Q_done, ones_(m, j))
                    wait(dve, res_done, ones_(m, j))
                wait(dve, out_tile, tiles(m, j - 1, t))
                dve.scalar_tensor_tensor(t_sb[:, t, :], q_ps[:, t, :], node_inv[j % 2][:, t:t + 1],
                                         res[j % 2][:, t, :], ALU.mult, ALU.add).then_inc(t_tile, 1)

            def split_r(m, j, k):
                wait(dve, r_hi_tile, tiles(m, j, k))
                wait(dve, Y_tile, tiles(m, j - 1, 1))
                dve.tensor_tensor(r_lo[:, 2 * k:2 * k + 2, :], r_ps[k],
                                  r_hi[:, 2 * k:2 * k + 2, :].bitcast(F32), ALU.subtract).then_inc(r_lo_tile, 1)

            def split_a(m, j):
                wait(dve, a_hi_done, ones_(m, j))
                wait(dve, Q_done, ones_(m, j - 2))
                dve.tensor_tensor(a_lo[j % 2][:, :, :], a_ps, a_hi[j % 2][:, :, :].bitcast(F32),
                                  ALU.subtract).then_inc(a_lo_done, 1)

            def rstd1_(m, j):
                wait(dve, sd1_done, ones_(m, j))
                wait(dve, y_tile, tiles(m, j - 1, 1))
                dve.reciprocal(rstd1[:, :], sd1[:, :]).then_inc(rstd1_done, 1)

            def project_out(m, j, t):
                if t == 0:
                    wait(dve, rstd1_done, ones_(m, j))
                wait(dve, Y_tile, tiles(m, j, t))
                wait(dve, y_lo_tile, tiles(m, j - 1, t))
                wait(dve, y_hi_tile, tiles(m, j - 1, t))
                dve.scalar_tensor_tensor(y[:, t, :], y_ps[t], rstd1[:, t:t + 1], beta_w2[:, :],
                                         ALU.mult, ALU.add).then_inc(y_tile, 1)

            def node_weight(m, j):
                wait(dve, D_done, ones_(m, j))
                wait(dve, node_inv_done, ones_(m, j - 1))
                dve.tensor_reduce(node_w[:, :], d_ps, mybir.AxisListType.X, ALU.add).then_inc(node_w_done, 1)

            def node_guard(m, j):
                wait(dve, node_w_done, ones_(m, j))
                dve.tensor_scalar(node_w1[:, :], node_w[:, :], TINY, None, ALU.max).then_inc(node_w1_done, 1)

            def node_recip(m, j):
                wait(dve, node_w1_done, ones_(m, j))
                dve.reciprocal(node_r[:, :], node_w1[:, :]).then_inc(node_r_done, 1)

            def node_inverse(m, j):
                wait(dve, node_r_done, ones_(m, j))
                wait(dve, t_tile, tiles(m, j - 2, 1))
                dve.scalar_tensor_tensor(node_inv[j % 2][:, :], node_w[:, :], 0.0, node_r[:, :],
                                         ALU.is_gt, ALU.mult).then_inc(node_inv_done, 1)

            def incidence(m, j, k):
                if k == 0:
                    wait(dve, T_done, ones_(m, j))
                    wait(dve, A_done, ones_(m, j - 1))
                    wait(dve, D_done, ones_(m, j - 1))
                    wait(dve, hb_lo_done, ones_(m, j - 1))
                    wait(dve, hb_hi_done, ones_(m, j - 1))
                    wait(dve, edge_n1_done, ones_(m, j - 1))
                dve.tensor_scalar(ht[:, k, :], t_ps[:, k, :], 0.0, None, ALU.not_equal, ALU.add,
                                  accum_out=edge_n[:, k:k + 1]).then_inc(ht_tile, 1)

            def edge_guard(m, j):
                wait(dve, ht_tile, tiles(m, j, 1))
                dve.tensor_scalar(edge_n1[:, :], edge_n[:, :], 1.0, None, ALU.max).then_inc(edge_n1_done, 1)

            def edge_recip(m, j):
                wait(dve, edge_n1_done, ones_(m, j))
                dve.reciprocal(edge_inv[:, :], edge_n1[:, :]).then_inc(edge_inv_done, 1)

            def split_p(m, j):
                wait(dve, p_hi_done, ones_(m, j))
                wait(dve, Z_tile, tiles(m, j - 1, 1))
                dve.tensor_tensor(p_lo[:, :, :], p_ps, p_hi[:, :, :].bitcast(F32),
                                  ALU.subtract).then_inc(p_lo_done, 1)

            def stats2(m, j, t):
                wait(dve, t_tile, tiles(m, j, t))
                dve.bn_stats(st2[:, t, :], t_sb[:, t, :]).then_inc(st2_tile, 1)

            def before_aggr2(m, j):
                wait(dve, st2_tile, tiles(m, j, 1))
                wait(dve, sd2_done, ones_(m, j - 1))
                wait(dve, shift2_done, ones_(m, j - 1))

            def aggr2(m, j):
                for t in range(CT):
                    dve.bn_aggr(mv2[:, t, :], st2[:, t, :]).then_inc(mv2_tile, 1)

            def rstd2_(m, j):
                wait(dve, sd2_done, ones_(m, j))
                wait(dve, out_tile, tiles(m, j - 1, 1))
                dve.reciprocal(rstd2[:, :], sd2[:, :]).then_inc(rstd2_done, 1)

            def shift2_(m, j):
                wait(dve, rstd2_done, ones_(m, j))
                dve.scalar_tensor_tensor(shift2[:, :], mv2[:, :, 0], -1.0, rstd2[:, :],
                                         ALU.mult, ALU.mult).then_inc(shift2_done, 1)

            def slot(m, j):
                if known(m, j - 1):
                    project_out(m, j - 1, 1)
                if known(m, j):
                    conv1_out(m, j, 0)
                    conv1_out(m, j, 1)
                    stats1(m, j, 0)
                if known(m, j - 1):
                    conv2_out(m, j - 1, 0)
                    conv2_out(m, j - 1, 1)
                if known(m, j):
                    stats1(m, j, 1)
                    split_r(m, j, 0)
                    before_aggr1(m, j)
                    split_r(m, j, 1)
                    aggr1(m, j)
                if known(m, j + 1):
                    split_a(m, j + 1)
                    node_weight(m, j + 1)
                if known(m, j - 1):
                    stats2(m, j - 1, 0)
                if known(m, j + 1):
                    node_guard(m, j + 1)
                if known(m, j - 1):
                    stats2(m, j - 1, 1)
                if known(m, j):
                    rstd1_(m, j)
                if known(m, j + 1):
                    node_recip(m, j + 1)
                if known(m, j - 1):
                    before_aggr2(m, j - 1)
                if known(m, j):
                    project_out(m, j, 0)
                if known(m, j - 1):
                    aggr2(m, j - 1)
                if known(m, j + 1):
                    node_inverse(m, j + 1)
                if known(m, j + 2):
                    incidence(m, j + 2, 0)
                    incidence(m, j + 2, 1)
                    edge_guard(m, j + 2)
                if known(m, j - 1):
                    rstd2_(m, j - 1)
                if known(m, j + 2):
                    edge_recip(m, j + 2)
                if known(m, j - 1):
                    shift2_(m, j - 1)
                if known(m, j + 1):
                    split_p(m, j + 1)

            dve.wait_ge(s_bias, 16 * (1 + CT))
            run(dve, slot, setup, setup2)

        @block.scalar
        def _(act):
            def setup2():
                act.wait_ge(s_w1T, 1)
                for d in range(DT):
                    act.copy(w1_hi[:, d, :], w1_ps[d][:, :]).then_inc(s_w1h, 1)
                act.wait_ge(s_w2T, 1)
                for k in range(HT_):
                    act.copy(w2_t[:, k, :], w2_ps[k // 2][:, k % 2, :]).then_inc(s_w2t, 1)
                act.wait_ge(s_w2c, HT_)
                act.copy(w2_hi[:, :, :], w2_c[:, :, :]).then_inc(s_w2h, 1)

            def y_high(m, j, t):
                wait(act, y_tile, tiles(m, j, t))
                wait(act, Q_done, ones_(m, j - 1))
                act.copy(y_hi[:, t, :], y[:, t, :]).then_inc(y_hi_tile, 1)

            def relu(m, j, t):
                wait(act, v_tile, tiles(m, j, t))
                wait(act, R_done, ones_(m, j - 1))
                wait(act, st1_tile, tiles(m, j - 1, t))
                act.activation(r[:, t, :], v[:, t, :], ACT.Relu).then_inc(r_tile, 1)

            def r_high(m, j, k):
                wait(act, R_done, ones_(m, j))
                wait(act, Y_tile, tiles(m, j - 1, 1))
                act.copy(r_hi[:, 2 * k:2 * k + 2, :], r_ps[k]).then_inc(r_hi_tile, 1)

            def deviation1(m, j):
                wait(act, mv1_tile, tiles(m, j, 1))
                wait(act, rstd1_done, ones_(m, j - 1))
                act.activation(sd1[:, :], mv1[:, :, 1], ACT.Sqrt, bias=eps[:, 0:1]).then_inc(sd1_done, 1)

            def a_high(m, j):
                wait(act, A_done, ones_(m, j))
                wait(act, Q_done, ones_(m, j - 2))
                act.copy(a_hi[j % 2][:, :, :], a_ps).then_inc(a_hi_done, 1)

            def p_high(m, j):
                wait(act, P_done, ones_(m, j))
                wait(act, Z_tile, tiles(m, j - 1, 1))
                act.copy(p_hi[:, :, :], p_ps).then_inc(p_hi_done, 1)

            def deviation2(m, j):
                wait(act, mv2_tile, tiles(m, j, 1))
                wait(act, rstd2_done, ones_(m, j - 1))
                act.activation(sd2[:, :], mv2[:, :, 1], ACT.Sqrt, bias=eps[:, 0:1]).then_inc(sd2_done, 1)

            def normalise(m, j, t):
                if t == 0:
                    wait(act, shift2_done, ones_(m, j))
                    wait(act, out_stored[j % 2], loads(m, j - 2))
                act.activation(out_sb[j % 2][:, t, :], t_sb[:, t, :], ACT.Identity,
                               bias=shift2[:, t:t + 1], scale=rstd2[:, t:t + 1]).then_inc(out_tile, 1)

            def x_high(m, j):
                wait(act, x_loaded[j % 2], loads(m, j))
                wait(act, P_done, ones_(m, j - 1))
                act.copy(x_hi[:, :, :], x_in[j % 2][:, :, :]).then_inc(x_hi_done, 1)

            def slot(m, j):
                if known(m, j - 1):
                    y_high(m, j - 1, 1)
                if known(m, j + 1):
                    x_high(m, j + 1)
                if known(m, j):
                    relu(m, j, 0)
                    relu(m, j, 1)
                    r_high(m, j, 0)
                    r_high(m, j, 1)
                if known(m, j + 1):
                    a_high(m, j + 1)
                if known(m, j):
                    deviation1(m, j)
                    y_high(m, j, 0)
                if known(m, j - 1):
                    deviation2(m, j - 1)
                if known(m, j + 1):
                    p_high(m, j + 1)
                if known(m, j - 1):
                    normalise(m, j - 1, 0)
                    normalise(m, j - 1, 1)

            act.wait_ge(s_const, 4)
            run(act, slot, None, setup2)

        @block.gpsimd
        def _(pool):
            def setup2():
                pool.wait_ge(s_gb, 1)
                for k in range(HT_):
                    pool.tensor_scalar(beta_rep[:, k, :], ones[:, :], gb_col[:, HT_ + k:HT_ + k + 1], 1.0,
                                       ALU.mult, ALU.mult).then_inc(s_brep, 1)

            def y_low(m, j, t):
                wait(pool, y_hi_tile, tiles(m, j, t))
                wait(pool, y_tile, tiles(m, j, t))
                wait(pool, Q_done, ones_(m, j - 1))
                pool.tensor_tensor(y_lo[:, t, :], y[:, t, :], y_hi[:, t, :].bitcast(F32),
                                   ALU.subtract).then_inc(y_lo_tile, 1)

            def hb_high(m, j):
                wait(pool, edge_inv_done, ones_(m, j))
                wait(pool, ht_tile, tiles(m, j, 1))
                wait(pool, A_done, ones_(m, j - 1))
                pool.tensor_tensor(hb_hi[:, :, :], ht[:, :, :].bitcast(F32),
                                   edge_inv[:, :].unsqueeze(2).broadcast_to([P, ET, C]),
                                   ALU.mult).then_inc(hb_hi_done, 1)

            def edge_split(m, j):
                wait(pool, edge_inv_done, ones_(m, j))
                pool.tensor_tensor(edge_inv_hi[:, :], edge_inv[:, :], ones[:, 0:ET],
                                   ALU.mult).then_inc(edge_hi_done, 1)
                wait(pool, edge_hi_done, ones_(m, j))
                pool.tensor_tensor(edge_inv_lo[:, :], edge_inv[:, :], edge_inv_hi[:, :].bitcast(F32),
                                   ALU.subtract).then_inc(edge_lo_done, 1)

            def hb_low(m, j):
                wait(pool, edge_lo_done, ones_(m, j))
                wait(pool, A_done, ones_(m, j - 1))
                pool.tensor_tensor(hb_lo[:, :, :], ht[:, :, :].bitcast(F32),
                                   edge_inv_lo[:, :].unsqueeze(2).broadcast_to([P, ET, C]),
                                   ALU.mult).then_inc(hb_lo_done, 1)

            def x_low(m, j):
                wait(pool, x_hi_done, ones_(m, j))
                wait(pool, x_loaded[j % 2], loads(m, j))
                wait(pool, P_done, ones_(m, j - 1))
                pool.tensor_tensor(x_lo[:, :, :], x_in[j % 2][:, :, :], x_hi[:, :, :].bitcast(F32),
                                   ALU.subtract).then_inc(x_lo_done, 1)

            def residual(m, j):
                wait(pool, x_loaded[j % 2], loads(m, j))
                wait(pool, res_done, ones_(m, j - 1))
                pool.tensor_tensor(res_b[:, :, :], x_in[j % 2][:, :, :], b2_all[:, :, :],
                                   ALU.add).then_inc(res_b_done, 1)
                wait(pool, res_b_done, ones_(m, j))
                wait(pool, t_tile, tiles(m, j - 2, 1))
                pool.tensor_tensor(res[j % 2][:, :, :], res_b[:, :, :], x_in[j % 2][:, :, :],
                                   ALU.add).then_inc(res_done, 1)

            def slot(m, j):
                if known(m, j - 1):
                    y_low(m, j - 1, 1)
                if known(m, j + 1):
                    hb_low(m, j + 1)
                    x_low(m, j + 1)
                    residual(m, j + 1)
                if known(m, j):
                    y_low(m, j, 0)
                if known(m, j + 2):
                    hb_high(m, j + 2)
                    edge_split(m, j + 2)

            pool.memset(ident[:, :], 0.0).then_inc(s_zeroed, 1)
            pool.memset(ones[:, :], 1.0).then_inc(s_const, 1)
            pool.wait_ge(s_zeroed, 1)
            pool.affine_select(out=ident[:, :], in_=ident[:, :], compare_op=ALU.not_equal, fill=1.0,
                               base=0, pattern=[[-1, P]], channel_multiplier=1).then_inc(s_const, 1)
            pool.memset(inv_dh[:, :], 1.0 / DH).then_inc(s_const, 1)
            pool.memset(eps[:, :], EPS).then_inc(s_const, 1)
            pool.wait_ge(s_const, 4)
            pool.wait_ge(s_bias, 16 * (1 + CT))
            run(pool, slot, None, setup2)


_INS = ["x", "adj", "L0_gnn_W1", "L0_gnn_b1", "L0_gnn_gamma", "L0_gnn_beta", "L0_gnn_W2", "L0_gnn_b2"]


def kernel(**inputs):
    import numpy as _np
    import concourse.bacc as _bacc
    from concourse import mybir as _mybir
    from concourse.bass_utils import run_bass_kernel_spmd as _run

    nc = _bacc.Bacc("TRN2", target_bir_lowering=False, num_devices=1)
    arrays, args = {}, []
    for name in _INS:
        a = _np.ascontiguousarray(inputs[name])
        arrays[f"in_{name}_dram"] = a
        args.append(nc.dram_tensor(f"in_{name}_dram", a.shape, _mybir.dt.from_np(a.dtype),
                                   kind="ExternalInput").ap())
    shape = arrays["in_x_dram"].shape
    args.append(nc.dram_tensor("out_0_dram", shape, _mybir.dt.from_np(_np.dtype("float32")),
                               kind="ExternalOutput").ap())
    hypergraph_resnorm_kernel(nc, *args)
    r = _run(nc, [arrays], core_ids=[0])
    return r.results[0]["out_0_dram"]
```

```python
from contextlib import ExitStack

import concourse.bass as bass
from concourse import mybir

ALU = mybir.AluOpType
ACT = mybir.ActivationFunctionType
F32 = mybir.dt.float32
F32R = mybir.dt.float32r
BF16 = mybir.dt.bfloat16
AX_X = mybir.AxisListType.X

P = 128
EPS = 1e-5
SUMS = 32
TINY = 1.1754944e-38


def hypergraph_resnorm_kernel(nc, x, adj, W1, b1, gamma, beta, W2, b2, out):
    N, C, DI = x.shape
    DH = W1.shape[0]
    DO = W2.shape[0]
    CT, ET, DT, HT_, OT = C // P, C // P, DI // P, DH // P, DO // P
    assert C == 2 * P and DI == DO == 2 * P and DH == 4 * P and N % 2 == 0 and N >= 12

    x_rows = x.rearrange("n (p t) d -> n p t d", t=CT)
    adj_rows = adj.rearrange("n (p t) e -> n p t e", t=CT)
    out_rows = out.rearrange("n (p t) d -> n p t d", t=CT)

    with ExitStack() as ctx:
        def sb(name, shape, dt=F32):
            return ctx.enter_context(nc.sbuf_tensor(name, shape, dt))

        def bank(name, shape):
            return ctx.enter_context(nc.psum_tensor(name, shape, F32))

        def sem(name):
            return ctx.enter_context(nc.semaphore(name))

        ident = sb("ident", [P, P])
        ident_b = sb("ident_b", [P, P], BF16)
        ones = sb("ones", [P, P])
        eps = sb("eps", [P, 1])
        w1_in = sb("w1_in", [P, HT_, DI])
        w2_in = sb("w2_in", [P, OT, DH])
        gamma_all = sb("gamma_all", [P, DH])
        beta_all = sb("beta_all", [P, DH])
        wrow_in = sb("wrow_in", [N, C])
        b1_all = sb("b1_all", [P, DH])
        b2_all = sb("b2_all", [P, DO])
        edge_w = sb("edge_w", [P, ET, N, 2], F32R)
        w1_hi = sb("w1_hi", [P, DT, DH], F32R)
        w1_lo = sb("w1_lo", [P, DT, DH], F32R)
        w2_g = sb("w2_g", [P, OT, DH])
        w2_part = sb("w2_part", [P, OT, DH // SUMS])
        w2_sum = sb("w2_sum", [P, OT])
        w2_shift = sb("w2_shift", [P, OT])
        w2_c = sb("w2_c", [P, OT, DH])
        w2_b = sb("w2_b", [P, OT, DH])
        beta_col = sb("beta_col", [P, OT])
        beta_rep = sb("beta_rep", [P, OT, P])
        w2_hi = sb("w2_hi", [P, HT_, DO], F32R)
        w2_lo = sb("w2_lo", [P, HT_, DO], F32R)
        beta_w2 = sb("beta_w2", [P, DO])

        x_in = [sb(f"x_in{j}", [P, CT, DI]) for j in range(2)]
        adj_in = [sb(f"adj_in{j}", [P, CT, C]) for j in range(2)]
        res = [sb(f"res{j}", [P, CT, DO]) for j in range(2)]
        t_sb = [sb(f"t_sb{j}", [P, CT, DO]) for j in range(2)]
        out_sb = [sb(f"out_sb{j}", [P, CT, DO]) for j in range(2)]
        a_hi = [sb(f"a_hi{j}", [P, CT, C], F32R) for j in range(2)]
        a_lo = [sb(f"a_lo{j}", [P, CT, C], F32R) for j in range(2)]
        node_inv = [sb(f"node_inv{j}", [P, CT]) for j in range(2)]

        h = sb("h", [P, CT, C], BF16)
        ht = sb("ht", [P, ET, C], F32R)
        edge_n = sb("edge_n", [P, ET])
        edge_n1 = sb("edge_n1", [P, ET])
        edge_inv = sb("edge_inv", [P, ET])
        edge_inv_hi = sb("edge_inv_hi", [P, ET], F32R)
        edge_inv_lo = sb("edge_inv_lo", [P, ET])
        hb_hi = sb("hb_hi", [P, ET, C + 2], F32R)
        hb_lo = sb("hb_lo", [P, ET, C], F32R)
        node_w = sb("node_w", [P, CT])
        node_w1 = sb("node_w1", [P, CT])
        node_r = sb("node_r", [P, CT])
        x_hi = sb("x_hi", [P, CT, DI], F32R)
        x_lo = sb("x_lo", [P, CT, DI], F32R)
        x2 = sb("x2", [P, CT, DO])
        p_hi = sb("p_hi", [P, DT, C], F32R)
        p_lo = sb("p_lo", [P, DT, C], F32R)
        v = sb("v", [P, CT, DH])
        r = sb("r", [P, CT, DH])
        st = sb("st", [P, 2 * CT, 6])
        mv = sb("mv", [P, 2 * CT, 2])
        sd = sb("sd", [P, 2 * CT])
        sd_inv = sb("sd_inv", [P, 2 * CT])
        newton_a = sb("newton_a", [P, 2 * CT])
        newton_b = sb("newton_b", [P, 2 * CT])
        rstd = sb("rstd", [P, 2 * CT])
        shift = sb("shift", [P, CT])
        spare = sb("spare", [P, 3])
        r_hi = sb("r_hi", [P, HT_, C], F32R)
        r_lo = sb("r_lo", [P, HT_, C], F32R)
        y = sb("y", [P, CT, DO])
        y_hi = sb("y_hi", [P, CT, DO], F32R)
        y_lo = sb("y_lo", [P, CT, DO], F32R)
        zr = [bank(f"zr{k}", [P, 512]) for k in range(2)]
        ys = [bank(f"ys{t}", [P, 512]) for t in range(2)]
        aps = bank("aps", [P, CT, 512])
        qs = bank("qs", [P, 512])
        ts = ctx.enter_context(nc.psum_tensor("ts", [P, 1024], BF16))
        z_ps = zr
        r_ps = [b[:, :].rearrange("p (k c) -> p k c", k=2) for b in zr]
        y_ps = [b[:, 0:DO] for b in ys]
        a_ps = aps[:, :, 0:C]
        d_ps = aps[:, :, C:C + 2]
        p_ps = aps[:, 0, :].rearrange("p (k c) -> p k c", k=DT)
        q_ps = qs[:, :].rearrange("p (t o) -> p t o", t=CT)
        t_ps = ts[:, 0:ET * C].rearrange("p (k c) -> p k c", k=ET)
        w1_ps = zr
        w2_ps = [b[:, :].rearrange("p (k o) -> p k o", k=2) for b in ys]
        wcol_ps = qs[:, DO:DO + ET * N].rearrange("p (k n) -> p k n", k=ET)
        beta_ps = qs[:, 0:DO]

        s_wrow = sem("s_edge_weights_loaded")
        s_w1 = sem("s_w1_loaded")
        s_w2 = sem("s_w2_loaded")
        s_gamma = sem("s_gamma_loaded")
        s_beta = sem("s_beta_loaded")
        s_b1 = sem("s_b1_loaded")
        s_b2 = sem("s_b2_loaded")
        s_zeroed = sem("s_zeroed")
        s_ones = sem("s_ones_made")
        s_const = sem("s_const_made")
        s_root = sem("s_root_taken")
        s_ewT = sem("s_edge_w_transposed")
        s_ewh = sem("s_edge_w_hi")
        s_ewl = sem("s_edge_w_lo")
        s_w1T = sem("s_w1_transposed")
        s_w1h = sem("s_w1_hi")
        s_w1l = sem("s_w1_lo")
        s_w2g = sem("s_w2_gamma")
        s_w2s = sem("s_w2_sums")
        s_w2m = sem("s_w2_means")
        s_w2c = sem("s_w2_centred")
        s_w2T = sem("s_w2_transposed")
        s_w2h = sem("s_w2_hi")
        s_w2l = sem("s_w2_lo")
        s_w2b = sem("s_w2_beta")
        s_bsum = sem("s_beta_sums")
        s_brep = sem("s_beta_rep")
        s_bT = sem("s_beta_w2_spread")
        s_bw2 = sem("s_beta_w2")

        x_loaded = [sem(f"x_loaded{j}") for j in range(2)]
        adj_loaded = [sem(f"adj_loaded{j}") for j in range(2)]
        out_stored = [sem(f"out_stored{j}") for j in range(2)]
        h_done = sem("h_done")
        edge_w_done = sem("edge_w_done")
        T_done = sem("T_done")
        A_tile = sem("A_tile")
        P_done = sem("P_done")
        Z_tile = sem("Z_tile")
        R_half = sem("R_half")
        Y_tile = sem("Y_tile")
        Q_done = sem("Q_done")
        ht_tile = sem("ht_tile")
        edge_n1_done = sem("edge_n1_done")
        edge_inv_done = sem("edge_inv_done")
        edge_hi_done = sem("edge_hi_done")
        edge_lo_done = sem("edge_lo_done")
        hb_hi_done = sem("hb_hi_done")
        hb_lo_done = sem("hb_lo_done")
        a_hi_tile = sem("a_hi_tile")
        a_lo_tile = sem("a_lo_tile")
        node_w_tile = sem("node_w_tile")
        node_w1_done = sem("node_w1_done")
        node_r_done = sem("node_r_done")
        node_inv_done = sem("node_inv_done")
        x_hi_done = sem("x_hi_done")
        x_lo_done = sem("x_lo_done")
        x2_done = sem("x2_done")
        res_done = sem("res_done")
        p_hi_done = sem("p_hi_done")
        p_lo_done = sem("p_lo_done")
        v_tile = sem("v_tile")
        r_tile = sem("r_tile")
        st1_tile = sem("st1_tile")
        r_hi_tile = sem("r_hi_tile")
        r_lo_tile = sem("r_lo_tile")
        y_tile = sem("y_tile")
        y_hi_tile = sem("y_hi_tile")
        y_lo_tile = sem("y_lo_tile")
        t_tile = sem("t_tile")
        st2_tile = sem("st2_tile")
        shift_done = sem("shift_done")
        out_tile = sem("out_tile")
        mv_done = sem("mv_done")
        sd_done = sem("sd_done")
        sd_inv_done = sem("sd_inv_done")
        newton_a_done = sem("newton_a_done")
        newton_b_done = sem("newton_b_done")
        rstd_done = sem("rstd_done")

        def known(m, j):
            return not isinstance(m, int) or 0 <= 2 * m + j < N

        def number(m, j):
            return 2 * m + j if isinstance(m, int) else None

        def ones_(m, j):
            return 2 * m + (j + 1)

        def tiles(m, j, t):
            return 4 * m + (2 * j + t + 1)

        def loads(m, j):
            return 16 * m + 16 * (j // 2 + 1)

        def wait(eng, s, value):
            if not isinstance(value, int) or value > 0:
                eng.wait_ge(s, value)

        def run(eng, slot, setup=None, ahead=2):
            slot(-1, 0)
            if setup:
                setup()
            slot(-1, 1)
            for m in range(2):
                slot(m, 0)
                slot(m, 1)
            whole = (N - ahead) // 2
            with eng.Fori(2, whole) as m:
                slot(m, 0)
                slot(m, 1)
            for m in range(whole, N // 2):
                slot(m, 0)
                slot(m, 1)
            slot(N // 2, 0)
            slot(N // 2, 1)

        block = ctx.enter_context(nc.Block())

        @block.sync
        def _(sp):
            def load_x(m, j):
                if known(m, j):
                    sp.dma_start(x_in[j % 2][:, :, :], x_rows[2 * m + j]).then_inc(x_loaded[j % 2], 16)

            def load_adj(m, j):
                if known(m, j):
                    sp.dma_start(adj_in[j % 2][:, :, :], adj_rows[2 * m + j]).then_inc(adj_loaded[j % 2], 16)

            def rows(a):
                return a.rearrange("(a d) -> a d", a=1).broadcast_to([P, a.shape[0]])

            load_adj(0, 0)
            sp.dma_start(wrow_in[:, :], adj[:, 0, :]).then_inc(s_wrow, 16)
            load_x(0, 0)
            sp.dma_start(w1_in[:, :, :], W1.rearrange("(k p) d -> p k d", p=P)).then_inc(s_w1, 16)
            sp.dma_start(w2_in[:, :, :], W2.rearrange("(k p) h -> p k h", p=P)).then_inc(s_w2, 16)
            sp.dma_start(gamma_all[:, :], rows(gamma)).then_inc(s_gamma, 16)
            load_adj(0, 1)
            sp.dma_start(b2_all[:, :], rows(b2)).then_inc(s_b2, 16)
            sp.dma_start(b1_all[:, :], rows(b1)).then_inc(s_b1, 16)
            sp.dma_start(beta_all[:, :], rows(beta)).then_inc(s_beta, 16)
            load_x(0, 1)

            def slot(m, j):
                if known(m, j + 4) and known(m, j + 2):
                    wait(sp, h_done, ones_(m, j + 2))
                    load_adj(m, j + 4)
                if known(m, j + 3) and known(m, j + 1):
                    wait(sp, x_hi_done, ones_(m, j + 1))
                    wait(sp, x_lo_done, ones_(m, j + 1))
                    wait(sp, x2_done, ones_(m, j + 1))
                    load_x(m, j + 3)
                if known(m, j - 2):
                    wait(sp, out_tile, tiles(m, j - 2, 1))
                    sp.dma_start(out_rows[2 * m + (j - 2)], out_sb[j % 2][:, :, :]) \
                      .then_inc(out_stored[j % 2], 16)

            run(sp, slot, ahead=4)
            sp.wait_ge(out_stored[0], 16 * (N // 2))
            sp.wait_ge(out_stored[1], 16 * (N // 2))

        @block.tensor
        def _(pe):
            def transpose_h(m, j):
                wait(pe, h_done, ones_(m, j))
                wait(pe, ht_tile, tiles(m, j - 1, 1))
                for t in range(CT):
                    for k in range(ET):
                        ins = pe.transpose(t_ps[:, k, t * P:(t + 1) * P], h[:, t, k * P:(k + 1) * P],
                                           ident_b[:, :])
                ins.then_inc(T_done, 1)

            def build_a(m, j):
                wait(pe, hb_hi_done, ones_(m, j))
                wait(pe, hb_lo_done, ones_(m, j))
                wait(pe, edge_w_done, ones_(m, j))
                wait(pe, p_lo_done, ones_(m, j - 1))
                wait(pe, node_w_tile, tiles(m, j - 1, 1))
                for t in range(CT):
                    at = slice(t * P, (t + 1) * P)
                    for k in range(ET):
                        pe.matmul(aps[:, t, 0:C + 2], ht[:, k, at], hb_hi[:, k, :], start=(k == 0),
                                  stop=False)
                        ins = pe.matmul(a_ps[:, t, :], ht[:, k, at], hb_lo[:, k, :], start=False,
                                        stop=(k == ET - 1))
                    ins.then_inc(A_tile, 1)

            def aggregate_x(m, j):
                wait(pe, x_hi_done, ones_(m, j))
                wait(pe, x_lo_done, ones_(m, j))
                wait(pe, a_hi_tile, tiles(m, j, 1))
                wait(pe, a_lo_tile, tiles(m, j, 0))
                wait(pe, node_w_tile, tiles(m, j, 0))
                n = j % 2
                for k in range(DT):
                    at = slice(k * P, (k + 1) * P)
                    for t in range(CT):
                        for xx in (x_hi, x_lo):
                            pe.matmul(p_ps[:, k, :], xx[:, t, at], a_hi[n][:, t, :],
                                      start=(t == 0 and xx is x_hi), stop=False)
                    for t in range(CT):
                        if k == 0 and t == 1:
                            wait(pe, a_lo_tile, tiles(m, j, 1))
                        ins = pe.matmul(p_ps[:, k, :], x_hi[:, t, at], a_lo[n][:, t, :], start=False,
                                        stop=(t == CT - 1))
                ins.then_inc(P_done, 1)

            def hidden(m, j):
                wait(pe, p_hi_done, ones_(m, j))
                wait(pe, r_lo_tile, tiles(m, j - 1, 1))
                for t in range(CT):
                    at = slice(t * P, (t + 1) * P)
                    for k in range(DT):
                        for w in (w1_hi, w1_lo):
                            pe.matmul(z_ps[t][:, :], p_hi[:, k, at], w[:, k, :],
                                      start=(k == 0 and w is w1_hi), stop=False)
                    if t == 0:
                        wait(pe, p_lo_done, ones_(m, j))
                    for k in range(DT):
                        ins = pe.matmul(z_ps[t][:, :], p_lo[:, k, at], w1_hi[:, k, :], start=False,
                                        stop=(k == DT - 1))
                    ins.then_inc(Z_tile, 1)

            def transpose_r(m, j):
                wait(pe, v_tile, tiles(m, j, 1))
                for t in range(CT):
                    wait(pe, r_tile, tiles(m, j, t))
                    for k in range(HT_):
                        ins = pe.transpose(r_ps[k // 2][:, k % 2, t * P:(t + 1) * P],
                                           r[:, t, k * P:(k + 1) * P], ident[:, :])
                        if t == CT - 1 and k % 2:
                            ins.then_inc(R_half, 1)

            def project(m, j, t):
                wait(pe, y_tile, tiles(m, j - 1, t))
                at = slice(t * P, (t + 1) * P)
                for k in range(HT_):
                    if t == 0 and k % 2 == 0:
                        wait(pe, r_hi_tile, tiles(m, j, k // 2))
                    for w in (w2_hi, w2_lo):
                        pe.matmul(y_ps[t], r_hi[:, k, at], w[:, k, :],
                                  start=(k == 0 and w is w2_hi), stop=False)
                for k in range(HT_):
                    if t == 0 and k % 2 == 0:
                        wait(pe, r_lo_tile, tiles(m, j, k // 2))
                    ins = pe.matmul(y_ps[t], r_lo[:, k, at], w2_hi[:, k, :], start=False,
                                    stop=(k == HT_ - 1))
                ins.then_inc(Y_tile, 1)

            def aggregate_y(m, j):
                wait(pe, t_tile, tiles(m, j - 1, 1))
                wait(pe, y_hi_tile, tiles(m, j, 1))
                n = j % 2
                for t in range(CT):
                    at = slice(t * P, (t + 1) * P)
                    for k in range(CT):
                        for a in (a_hi, a_lo):
                            pe.matmul(q_ps[:, t, :], a[n][:, k, at], y_hi[:, k, :],
                                      start=(k == 0 and a is a_hi), stop=False)
                    if t == 0:
                        wait(pe, y_lo_tile, tiles(m, j, 1))
                    for k in range(CT):
                        ins = pe.matmul(q_ps[:, t, :], a_hi[n][:, k, at], y_lo[:, k, :], start=False,
                                        stop=(k == CT - 1))
                ins.then_inc(Q_done, 1)

            def setup():
                pe.wait_ge(s_wrow, 16)
                for k in range(ET):
                    ins = pe.transpose(wcol_ps[:, k, :], wrow_in[:, k * P:(k + 1) * P], ident[0:N, 0:N])
                ins.then_inc(s_ewT, 1)
                pe.wait_ge(s_w1, 16)
                for d in range(DT):
                    for k in range(HT_):
                        ins = pe.transpose(w1_ps[d][:, k * P:(k + 1) * P], w1_in[:, k, d * P:(d + 1) * P],
                                           ident[:, :])
                    ins.then_inc(s_w1T, 1)
                pe.wait_ge(s_ewl, 1)

            def setup_w2():
                pe.wait_ge(s_w2c, OT)
                for k in range(HT_):
                    for o in range(OT):
                        ins = pe.transpose(w2_ps[k // 2][:, k % 2, o * P:(o + 1) * P],
                                           w2_c[:, o, k * P:(k + 1) * P], ident[:, :])
                    if k % 2:
                        ins.then_inc(s_w2T, 1)

            def setup_beta():
                pe.wait_ge(s_brep, OT)
                for o in range(OT):
                    ins = pe.transpose(beta_ps[:, o * P:(o + 1) * P], beta_rep[:, o, :], ident[:, :])
                ins.then_inc(s_bT, 1)

            def slot(m, j):
                if known(m, j):
                    if number(m, j) == 0:
                        pe.wait_ge(s_w1h, DT)
                        pe.wait_ge(s_w1l, DT)
                    hidden(m, j)
                if number(m, j) == 0:
                    setup_w2()
                if known(m, j - 1):
                    if number(m, j) == 1:
                        pe.wait_ge(s_bw2, 1)
                    aggregate_y(m, j - 1)
                if known(m, j + 1):
                    build_a(m, j + 1)
                if known(m, j):
                    transpose_r(m, j)
                if known(m, j + 2):
                    transpose_h(m, j + 2)
                if known(m, j + 1):
                    aggregate_x(m, j + 1)
                if number(m, j) == 0:
                    setup_beta()
                    pe.wait_ge(s_w2h, 2)
                    pe.wait_ge(s_w2l, 2)
                if known(m, j):
                    project(m, j, 0)
                    project(m, j, 1)

            pe.wait_ge(s_const, 3)
            run(pe, slot, setup)

        @block.vector
        def _(dve):
            def setup():
                dve.wait_ge(s_ewT, 1)
                dve.tensor_copy(edge_w[:, :, :, 0], wcol_ps).then_inc(s_ewh, 1)
                dve.wait_ge(s_ewh, 1)
                dve.tensor_tensor(edge_w[:, :, :, 1], wcol_ps, edge_w[:, :, :, 0].bitcast(F32),
                                  ALU.subtract).then_inc(s_ewl, 1)
                edge_weight(0, 0)
                for d in range(DT):
                    dve.wait_ge(s_w1h, d + 1)
                    dve.tensor_tensor(w1_lo[:, d, :], w1_ps[d][:, :], w1_hi[:, d, :].bitcast(F32),
                                      ALU.subtract).then_inc(s_w1l, 1)

            def setup_w2_sums():
                dve.wait_ge(s_w2g, OT)
                dve.tensor_reduce(w2_part[:, :, :], w2_g[:, :, :].rearrange("p o (a b) -> p o a b", b=SUMS),
                                  AX_X, ALU.add).then_inc(s_w2s, 1)

            def setup_w2_centre():
                dve.wait_ge(s_w2s, 1)
                dve.tensor_reduce(w2_sum[:, :], w2_part[:, :, :], AX_X, ALU.add).then_inc(s_w2s, 1)
                dve.wait_ge(s_w2s, 2)
                dve.tensor_scalar(w2_shift[:, :], w2_sum[:, :], -1.0 / DH, None, ALU.mult).then_inc(s_w2m, 1)
                dve.wait_ge(s_w2m, 1)
                for o in range(OT):
                    dve.tensor_scalar(w2_c[:, o, :], w2_g[:, o, :], w2_shift[:, o:o + 1], None,
                                      ALU.add).then_inc(s_w2c, 1)

            def setup_w2():
                for k in range(2):
                    dve.wait_ge(s_w2h, k + 1)
                    dve.tensor_tensor(w2_lo[:, 2 * k:2 * k + 2, :], w2_ps[k],
                                      w2_hi[:, 2 * k:2 * k + 2, :].bitcast(F32),
                                      ALU.subtract).then_inc(s_w2l, 1)

            def setup_beta_row():
                dve.wait_ge(s_bT, 1)
                dve.tensor_copy(beta_w2[:, :], beta_ps).then_inc(s_bw2, 1)

            def conv1_out(m, j, t):
                if t == 0:
                    wait(dve, node_inv_done, ones_(m, j))
                    wait(dve, R_half, tiles(m, j - 1, 1))
                    if number(m, j) == 0:
                        dve.wait_ge(s_b1, 16)
                wait(dve, r_tile, tiles(m, j - 1, t))
                wait(dve, Z_tile, tiles(m, j, t))
                dve.scalar_tensor_tensor(v[:, t, :], z_ps[t][:, :], node_inv[j % 2][:, t:t + 1],
                                         b1_all[:, :], ALU.mult, ALU.add).then_inc(v_tile, 1)

            def stats1(m, j, t):
                wait(dve, r_tile, tiles(m, j, t))
                wait(dve, mv_done, ones_(m, j - 1))
                dve.bn_stats(st[:, t, :], r[:, t, :]).then_inc(st1_tile, 1)

            def stats2(m, j, t):
                wait(dve, t_tile, tiles(m, j, t))
                wait(dve, mv_done, ones_(m, j + 1))
                dve.bn_stats(st[:, CT + t, :], t_sb[j % 2][:, t, :]).then_inc(st2_tile, 1)

            def columns(m, j):
                return (0 if known(m, j) else CT), (2 * CT if known(m, j - 2) else CT)

            def before_means(m, j):
                if known(m, j):
                    wait(dve, st1_tile, tiles(m, j, 1))
                if known(m, j - 2):
                    wait(dve, st2_tile, tiles(m, j - 2, 1))
                wait(dve, sd_done, ones_(m, j - 1))
                wait(dve, newton_a_done, ones_(m, j - 1))
                wait(dve, shift_done, ones_(m, j - 3))

            def means(m, j):
                a, b = columns(m, j)
                for c in range(a, b):
                    ins = dve.bn_aggr(mv[:, c, :], st[:, c, :])
                ins.then_inc(mv_done, 1)

            def invert(m, j):
                a, b = columns(m, j)
                wait(dve, sd_done, ones_(m, j))
                wait(dve, rstd_done, ones_(m, j - 1))
                dve.reciprocal(sd_inv[:, a:b], sd[:, a:b]).then_inc(sd_inv_done, 1)

            def newton1(m, j):
                a, b = columns(m, j)
                wait(dve, sd_inv_done, ones_(m, j))
                wait(dve, newton_b_done, ones_(m, j - 1))
                dve.scalar_tensor_tensor(newton_a[:, a:b], mv[:, a:b, 1], EPS, sd_inv[:, a:b],
                                         ALU.add, ALU.mult).then_inc(newton_a_done, 1)

            def newton2(m, j):
                a, b = columns(m, j)
                wait(dve, newton_a_done, ones_(m, j))
                wait(dve, rstd_done, ones_(m, j - 1))
                dve.scalar_tensor_tensor(newton_b[:, a:b], newton_a[:, a:b], -0.5, sd_inv[:, a:b],
                                         ALU.mult, ALU.mult).then_inc(newton_b_done, 1)

            def newton3(m, j):
                a, b = columns(m, j)
                wait(dve, newton_b_done, ones_(m, j))
                if known(m, j - 1):
                    wait(dve, y_tile, tiles(m, j - 1, 1))
                wait(dve, out_tile, tiles(m, j - 3, 1))
                dve.scalar_tensor_tensor(rstd[:, a:b], newton_b[:, a:b], 1.5, sd_inv[:, a:b],
                                         ALU.add, ALU.mult).then_inc(rstd_done, 1)

            def shifts(m, j):
                wait(dve, rstd_done, ones_(m, j))
                wait(dve, out_tile, tiles(m, j - 3, 1))
                dve.scalar_tensor_tensor(shift[:, :], mv[:, CT:, 0], -1.0, rstd[:, CT:],
                                         ALU.mult, ALU.mult).then_inc(shift_done, 1)

            def conv2_out(m, j, t):
                if t == 0:
                    wait(dve, Q_done, ones_(m, j))
                    wait(dve, res_done, ones_(m, j))
                wait(dve, out_tile, tiles(m, j - 2, t))
                dve.scalar_tensor_tensor(t_sb[j % 2][:, t, :], q_ps[:, t, :], node_inv[j % 2][:, t:t + 1],
                                         res[j % 2][:, t, :], ALU.mult, ALU.add).then_inc(t_tile, 1)

            def split_r(m, j, k):
                wait(dve, r_hi_tile, tiles(m, j, k))
                wait(dve, Y_tile, tiles(m, j - 1, 1))
                dve.tensor_tensor(r_lo[:, 2 * k:2 * k + 2, :], r_ps[k],
                                  r_hi[:, 2 * k:2 * k + 2, :].bitcast(F32), ALU.subtract).then_inc(r_lo_tile, 1)

            def split_a(m, j, t):
                wait(dve, a_hi_tile, tiles(m, j, t))
                if t == 0:
                    wait(dve, Q_done, ones_(m, j - 2))
                dve.tensor_tensor(a_lo[j % 2][:, t, :], a_ps[:, t, :], a_hi[j % 2][:, t, :].bitcast(F32),
                                  ALU.subtract).then_inc(a_lo_tile, 1)

            def project_out(m, j, t):
                if t == 0:
                    wait(dve, rstd_done, ones_(m, j))
                if number(m, j) == 0:
                    dve.wait_ge(s_bw2, 1)
                wait(dve, Y_tile, tiles(m, j, t))
                wait(dve, y_lo_tile, tiles(m, j - 1, t))
                wait(dve, y_hi_tile, tiles(m, j - 1, t))
                dve.scalar_tensor_tensor(y[:, t, :], y_ps[t], rstd[:, t:t + 1], beta_w2[:, :],
                                         ALU.mult, ALU.add).then_inc(y_tile, 1)

            def node_weight(m, j, t):
                wait(dve, a_hi_tile, tiles(m, j, t))
                wait(dve, node_inv_done, ones_(m, j - 1))
                dve.tensor_reduce(node_w[:, t:t + 1], d_ps[:, t, :], AX_X, ALU.add).then_inc(node_w_tile, 1)

            def node_guard(m, j):
                wait(dve, node_w_tile, tiles(m, j, 1))
                dve.tensor_scalar(node_w1[:, :], node_w[:, :], TINY, None, ALU.max).then_inc(node_w1_done, 1)

            def node_recip(m, j):
                wait(dve, node_w1_done, ones_(m, j))
                dve.reciprocal(node_r[:, :], node_w1[:, :]).then_inc(node_r_done, 1)

            def node_inverse(m, j):
                wait(dve, node_r_done, ones_(m, j))
                wait(dve, t_tile, tiles(m, j - 2, 1))
                dve.scalar_tensor_tensor(node_inv[j % 2][:, :], node_w[:, :], 0.0, node_r[:, :],
                                         ALU.is_gt, ALU.mult).then_inc(node_inv_done, 1)

            def incidence(m, j):
                wait(dve, adj_loaded[j % 2], loads(m, j))
                wait(dve, T_done, ones_(m, j - 1))
                dve.tensor_scalar(h[:, :, :], adj_in[j % 2][:, :, :], 0.0, None,
                                  ALU.not_equal).then_inc(h_done, 1)

            def edge_weight(m, j):
                if number(m, j) == 0:
                    dve.wait_ge(s_ewl, 1)
                wait(dve, A_tile, tiles(m, j - 1, 1))
                if isinstance(m, int):
                    w = edge_w[:, :, 2 * m + j, :]
                else:
                    w = edge_w[:, :, bass.ds(2 * m + j, 1), :].rearrange("p k n h -> p k (n h)")
                dve.tensor_scalar(hb_hi[:, :, C:C + 2], w.bitcast(F32), 1.0, None, ALU.mult) \
                   .then_inc(edge_w_done, 1)

            def edge_guard(m, j):
                wait(dve, ht_tile, tiles(m, j, 1))
                dve.tensor_scalar(edge_n1[:, :], edge_n[:, :], 1.0, None, ALU.max).then_inc(edge_n1_done, 1)

            def edge_recip(m, j):
                wait(dve, edge_n1_done, ones_(m, j))
                dve.reciprocal(edge_inv[:, :], edge_n1[:, :]).then_inc(edge_inv_done, 1)

            def edge_split(m, j):
                wait(dve, edge_inv_done, ones_(m, j))
                dve.tensor_tensor(edge_inv_hi[:, :], edge_inv[:, :], ones[:, 0:ET],
                                   ALU.mult).then_inc(edge_hi_done, 1)
                wait(dve, edge_hi_done, ones_(m, j))
                dve.tensor_tensor(edge_inv_lo[:, :], edge_inv[:, :], edge_inv_hi[:, :].bitcast(F32),
                                   ALU.subtract).then_inc(edge_lo_done, 1)

            def hb_low(m, j):
                wait(dve, edge_lo_done, ones_(m, j))
                wait(dve, A_tile, tiles(m, j - 1, 1))
                dve.tensor_tensor(hb_lo[:, :, :], ht[:, :, :].bitcast(F32),
                                   edge_inv_lo[:, :].unsqueeze(2).broadcast_to([P, ET, C]),
                                   ALU.mult).then_inc(hb_lo_done, 1)

            def split_p(m, j):
                wait(dve, p_hi_done, ones_(m, j))
                wait(dve, Z_tile, tiles(m, j - 1, 1))
                dve.tensor_tensor(p_lo[:, :, :], p_ps, p_hi[:, :, :].bitcast(F32),
                                  ALU.subtract).then_inc(p_lo_done, 1)

            def slot(m, j):
                i = number(m, j)
                rows = known(m, j) or known(m, j - 2)
                last = known(m, j - 1) and not known(m, j)
                if known(m, j + 1) and i != -1:
                    edge_weight(m, j + 1)
                if known(m, j + 2):
                    incidence(m, j + 2)
                if known(m, j):
                    conv1_out(m, j, 0)
                    conv1_out(m, j, 1)
                    stats1(m, j, 0)
                    if i != 0:
                        stats1(m, j, 1)
                if known(m, j + 1):
                    split_a(m, j + 1, 0)
                    node_weight(m, j + 1, 0)
                    split_a(m, j + 1, 1)
                    node_weight(m, j + 1, 1)
                if i == 0:
                    setup_w2()
                    stats1(m, j, 1)
                if rows:
                    before_means(m, j)
                if known(m, j - 1) and not last:
                    conv2_out(m, j - 1, 0)
                elif rows:
                    at = max(0, i - N + 1)
                    dve.memset(spare[:, at:at + 1], 0.0)
                if rows:
                    means(m, j)
                if known(m, j):
                    split_r(m, j, 0)
                if rows:
                    invert(m, j)
                if known(m, j):
                    split_r(m, j, 1)
                if i == 0:
                    setup_beta_row()
                if rows:
                    newton1(m, j)
                if known(m, j - 1) and not last:
                    conv2_out(m, j - 1, 1)
                if rows:
                    newton2(m, j)
                if known(m, j + 2):
                    edge_guard(m, j + 2)
                if known(m, j + 1):
                    node_guard(m, j + 1)
                if rows:
                    newton3(m, j)
                if known(m, j + 2):
                    edge_recip(m, j + 2)
                if i == -2:
                    edge_split(m, j + 2)
                    hb_low(m, j + 2)
                if known(m, j + 1):
                    node_recip(m, j + 1)
                if i == -1:
                    setup_w2_sums()
                if known(m, j):
                    project_out(m, j, 0)
                if known(m, j + 1):
                    split_p(m, j + 1)
                if i == -1:
                    setup_w2_centre()
                if known(m, j):
                    project_out(m, j, 1)
                if known(m, j - 2):
                    shifts(m, j)
                if known(m, j + 1):
                    node_inverse(m, j + 1)
                if last:
                    conv2_out(m, j - 1, 0)
                    conv2_out(m, j - 1, 1)
                if known(m, j - 1):
                    stats2(m, j - 1, 0)
                    stats2(m, j - 1, 1)

            run(dve, slot, setup)

        @block.scalar
        def _(act):
            def setup():
                for d in range(DT):
                    act.wait_ge(s_w1T, d + 1)
                    act.copy(w1_hi[:, d, :], w1_ps[d][:, :]).then_inc(s_w1h, 1)

            def setup_w2():
                for k in range(2):
                    act.wait_ge(s_w2T, k + 1)
                    act.copy(w2_hi[:, 2 * k:2 * k + 2, :], w2_ps[k]).then_inc(s_w2h, 1)

            def setup_beta():
                act.wait_ge(s_w2b, OT)
                for o in range(OT):
                    act.activation(w2_b[:, o, :], w2_b[:, o, :], ACT.Copy,
                                   accum_out=beta_col[:, o:o + 1]).then_inc(s_bsum, 1)

            def incidence(m, j, k):
                if k == 0:
                    wait(act, T_done, ones_(m, j))
                    wait(act, A_tile, tiles(m, j - 1, 1))
                    wait(act, hb_lo_done, ones_(m, j - 1))
                    wait(act, hb_hi_done, ones_(m, j - 1))
                    wait(act, edge_n1_done, ones_(m, j - 1))
                act.activation(ht[:, k, :], t_ps[:, k, :], ACT.Copy,
                               accum_out=edge_n[:, k:k + 1]).then_inc(ht_tile, 1)

            def y_high(m, j, t):
                wait(act, y_tile, tiles(m, j, t))
                wait(act, Q_done, ones_(m, j - 1))
                act.copy(y_hi[:, t, :], y[:, t, :]).then_inc(y_hi_tile, 1)

            def relu(m, j, t):
                wait(act, v_tile, tiles(m, j, t))
                wait(act, R_half, tiles(m, j - 1, 1))
                wait(act, st1_tile, tiles(m, j - 1, t))
                act.activation(r[:, t, :], v[:, t, :], ACT.Relu).then_inc(r_tile, 1)

            def r_high(m, j, k):
                wait(act, R_half, tiles(m, j, k))
                wait(act, Y_tile, tiles(m, j - 1, 1))
                act.copy(r_hi[:, 2 * k:2 * k + 2, :], r_ps[k]).then_inc(r_hi_tile, 1)

            def deviations(m, j):
                a, b = (0 if known(m, j) else CT), (2 * CT if known(m, j - 2) else CT)
                wait(act, mv_done, ones_(m, j))
                wait(act, sd_inv_done, ones_(m, j - 1))
                act.activation(sd[:, a:b], mv[:, a:b, 1], ACT.Sqrt, bias=eps[:, 0:1]).then_inc(sd_done, 1)

            def a_high(m, j, t):
                wait(act, A_tile, tiles(m, j, t))
                if t == 0:
                    wait(act, Q_done, ones_(m, j - 2))
                act.copy(a_hi[j % 2][:, t, :], a_ps[:, t, :]).then_inc(a_hi_tile, 1)

            def p_high(m, j):
                wait(act, P_done, ones_(m, j))
                wait(act, Z_tile, tiles(m, j - 1, 1))
                act.copy(p_hi[:, :, :], p_ps).then_inc(p_hi_done, 1)

            def normalise(m, j, t):
                if t == 0:
                    wait(act, shift_done, ones_(m, j))
                    wait(act, out_stored[j % 2], loads(m, j - 2))
                act.activation(out_sb[j % 2][:, t, :], t_sb[j % 2][:, t, :], ACT.Identity,
                               bias=shift[:, t:t + 1], scale=rstd[:, CT + t:CT + t + 1]).then_inc(out_tile, 1)

            def x_high(m, j):
                wait(act, x_loaded[j % 2], loads(m, j))
                wait(act, P_done, ones_(m, j - 1))
                act.copy(x_hi[:, :, :], x_in[j % 2][:, :, :]).then_inc(x_hi_done, 1)

            def double(m, j):
                wait(act, x_loaded[j % 2], loads(m, j))
                wait(act, res_done, ones_(m, j - 1))
                act.activation(x2[:, :, :], x_in[j % 2][:, :, :], ACT.Copy, scale=2.0).then_inc(x2_done, 1)

            def slot(m, j):
                i = number(m, j)
                if known(m, j):
                    relu(m, j, 0)
                if known(m, j + 1) and i != -1:
                    x_high(m, j + 1)
                if known(m, j):
                    relu(m, j, 1)
                if known(m, j + 1):
                    a_high(m, j + 1, 0)
                    a_high(m, j + 1, 1)
                if i == 0:
                    setup_w2()
                if known(m, j):
                    r_high(m, j, 0)
                    r_high(m, j, 1)
                if known(m, j) or known(m, j - 2):
                    deviations(m, j)
                if known(m, j + 2):
                    incidence(m, j + 2, 0)
                    incidence(m, j + 2, 1)
                if known(m, j + 1):
                    p_high(m, j + 1)
                if i == -2:
                    x_high(m, j + 2)
                if i == -1:
                    setup_beta()
                if known(m, j + 1):
                    double(m, j + 1)
                if known(m, j):
                    y_high(m, j, 0)
                    y_high(m, j, 1)
                if known(m, j - 2):
                    normalise(m, j - 2, 0)
                    normalise(m, j - 2, 1)

            act.wait_ge(s_const, 3)
            act.activation(sd[:, :], ones[:, 0:2 * CT], ACT.Sqrt, bias=eps[:, 0:1]).then_inc(s_root, 1)
            act.wait_ge(s_root, 1)
            run(act, slot, setup)

        @block.gpsimd
        def _(pool):
            def setup_w2():
                pool.wait_ge(s_w2, 16)
                pool.wait_ge(s_gamma, 16)
                for o in range(OT):
                    pool.tensor_tensor(w2_g[:, o, :], w2_in[:, o, :], gamma_all[:, :],
                                       ALU.mult).then_inc(s_w2g, 1)

            def setup_beta():
                pool.wait_ge(s_beta, 16)
                for o in range(OT):
                    pool.tensor_tensor(w2_b[:, o, :], w2_in[:, o, :], beta_all[:, :],
                                       ALU.mult).then_inc(s_w2b, 1)

            def setup_beta_rep():
                pool.wait_ge(s_bsum, 2)
                for o in range(OT):
                    pool.tensor_scalar(beta_rep[:, o, :], ones[:, :], beta_col[:, o:o + 1], 1.0,
                                       ALU.mult, ALU.mult).then_inc(s_brep, 1)

            def y_low(m, j, t):
                wait(pool, y_hi_tile, tiles(m, j, t))
                wait(pool, y_tile, tiles(m, j, t))
                wait(pool, Q_done, ones_(m, j - 1))
                pool.tensor_tensor(y_lo[:, t, :], y[:, t, :], y_hi[:, t, :].bitcast(F32),
                                   ALU.subtract).then_inc(y_lo_tile, 1)

            def hb_high(m, j):
                wait(pool, edge_inv_done, ones_(m, j))
                wait(pool, ht_tile, tiles(m, j, 1))
                wait(pool, A_tile, tiles(m, j - 1, 1))
                pool.tensor_tensor(hb_hi[:, :, 0:C], ht[:, :, :].bitcast(F32),
                                   edge_inv[:, :].unsqueeze(2).broadcast_to([P, ET, C]),
                                   ALU.mult).then_inc(hb_hi_done, 1)

            def edge_split(m, j):
                wait(pool, edge_inv_done, ones_(m, j))
                pool.tensor_tensor(edge_inv_hi[:, :], edge_inv[:, :], ones[:, 0:ET],
                                   ALU.mult).then_inc(edge_hi_done, 1)
                wait(pool, edge_hi_done, ones_(m, j))
                pool.tensor_tensor(edge_inv_lo[:, :], edge_inv[:, :], edge_inv_hi[:, :].bitcast(F32),
                                   ALU.subtract).then_inc(edge_lo_done, 1)

            def hb_low(m, j):
                wait(pool, edge_lo_done, ones_(m, j))
                wait(pool, A_tile, tiles(m, j - 1, 1))
                pool.tensor_tensor(hb_lo[:, :, :], ht[:, :, :].bitcast(F32),
                                   edge_inv_lo[:, :].unsqueeze(2).broadcast_to([P, ET, C]),
                                   ALU.mult).then_inc(hb_lo_done, 1)

            def x_low(m, j):
                wait(pool, x_hi_done, ones_(m, j))
                wait(pool, x_loaded[j % 2], loads(m, j))
                wait(pool, P_done, ones_(m, j - 1))
                pool.tensor_tensor(x_lo[:, :, :], x_in[j % 2][:, :, :], x_hi[:, :, :].bitcast(F32),
                                   ALU.subtract).then_inc(x_lo_done, 1)

            def residual(m, j):
                if number(m, j) == 0:
                    pool.wait_ge(s_b2, 16)
                wait(pool, x2_done, ones_(m, j))
                wait(pool, t_tile, tiles(m, j - 2, 1))
                pool.tensor_tensor(res[j % 2][:, :, :], x2[:, :, :],
                                   b2_all[:, :].unsqueeze(1).broadcast_to([P, CT, DO]),
                                   ALU.add).then_inc(res_done, 1)

            def slot(m, j):
                i = number(m, j)
                if known(m, j + 1) and i != -1:
                    hb_low(m, j + 1)
                    x_low(m, j + 1)
                if i == -1:
                    setup_w2()
                    setup_beta()
                if i == 0:
                    setup_beta_rep()
                if known(m, j):
                    residual(m, j)
                if known(m, j + 2):
                    hb_high(m, j + 2)
                if i == -2:
                    x_low(m, j + 2)
                elif known(m, j + 2):
                    edge_split(m, j + 2)
                if known(m, j):
                    y_low(m, j, 0)
                    y_low(m, j, 1)

            pool.memset(ident[:, :], 0.0).then_inc(s_zeroed, 1)
            pool.memset(ones[:, :], 1.0).then_inc(s_ones, 1)
            pool.wait_ge(s_zeroed, 1)
            pool.affine_select(out=ident[:, :], in_=ident[:, :], compare_op=ALU.not_equal, fill=1.0,
                               base=0, pattern=[[-1, P]], channel_multiplier=1).then_inc(s_const, 1)
            pool.memset(eps[:, :], EPS).then_inc(s_const, 1)
            pool.wait_ge(s_const, 2)
            pool.wait_ge(s_ones, 1)
            pool.tensor_copy(ident_b[:, :], ident[:, :]).then_inc(s_const, 1)
            run(pool, slot)


_INS = ["x", "adj", "L0_gnn_W1", "L0_gnn_b1", "L0_gnn_gamma", "L0_gnn_beta", "L0_gnn_W2", "L0_gnn_b2"]


def kernel(**inputs):
    import numpy as _np
    import concourse.bacc as _bacc
    from concourse import mybir as _mybir
    from concourse.bass_utils import run_bass_kernel_spmd as _run

    nc = _bacc.Bacc("TRN2", target_bir_lowering=False, num_devices=1)
    arrays, args = {}, []
    for name in _INS:
        a = _np.ascontiguousarray(inputs[name])
        arrays[f"in_{name}_dram"] = a
        args.append(nc.dram_tensor(f"in_{name}_dram", a.shape, _mybir.dt.from_np(a.dtype),
                                   kind="ExternalInput").ap())
    shape = arrays["in_x_dram"].shape
    args.append(nc.dram_tensor("out_0_dram", shape, _mybir.dt.from_np(_np.dtype("float32")),
                               kind="ExternalOutput").ap())
    hypergraph_resnorm_kernel(nc, *args)
    r = _run(nc, [arrays], core_ids=[0])
    return r.results[0]["out_0_dram"]
```
